# Optimizing a Trainium2 kernel written in Bass

```python
import numpy as np
import jax
import jax.numpy as jnp

def _softmax(x, axis=-1):
    return jax.nn.softmax(x, axis=axis)
def _gelu(x):
    return jax.nn.gelu(x, approximate=True)
def _silu(x):
    return jax.nn.silu(x)
def _sigmoid(x):
    return jax.nn.sigmoid(x)
def _layernorm(x, axis=-1, eps=1e-5):
    m = jnp.mean(x, axis=axis, keepdims=True)
    v = jnp.var(x, axis=axis, keepdims=True)
    return (x - m) / jnp.sqrt(v + eps)
def _scatter_add(tgt, idx, src, axis=0):
    return tgt.at[idx].add(src)
def _segment_sum(src, seg, n):
    return jax.ops.segment_sum(src, seg, n)

kernel_name = 'mk_adj_resnorm_d2_adj_512_242202'

def setup_inputs(seed: int = 0):
    np.random.seed(seed)
    _w = jnp.asarray
    def _rec_inputs():
        import jax
        import jax.numpy as jnp
        _gk = jax.random.key(seed)
        x = -0.0005207 + 1.001 * jax.random.normal(jax.random.fold_in(_gk, 1), (4096, 512), jnp.float32)
        _w = (1.0 + jnp.arange(4096, dtype=jnp.float32)) ** -0.5
        _w = _w / _w.mean()
        _pij = jnp.clip(0.0078125 * _w[:, None] * _w[None, :], 0.0, 1.0)
        _a = jax.random.uniform(jax.random.fold_in(_gk, 2), (4096, 4096)) < _pij
        _af = _a.astype(jnp.float32)
        adj = _af
        return x, adj
    x, adj = _rec_inputs()
    def _L0_gnn_setup():
        import jax, jax.numpy as jnp
        import numpy as np
        NHEADS = 8
        OUT_FEATURES = 64
        ALPHA = 0.2
        NEG_INF = -10000000000.0
        key = jax.random.key(seed)
        k1, k2, k3, k4, k5 = jax.random.split(key, 5)
        n, in_f = (4096, 512)
        x = jax.random.normal(k1, (n, in_f), dtype=jnp.float32)
        adj = (jax.random.uniform(k2, (n, n)) < 0.01).astype(jnp.float32)
        weight = jax.random.normal(k3, (in_f, NHEADS * OUT_FEATURES), dtype=jnp.float32) * (1.0 / np.sqrt(in_f))
        linear_i = jax.random.normal(k4, (1, NHEADS, OUT_FEATURES), dtype=jnp.float32) * 0.1
        linear_j = jax.random.normal(k5, (1, NHEADS, OUT_FEATURES), dtype=jnp.float32) * 0.1
        return {'x': x, 'adj': adj, 'weight': weight, 'linear_i': linear_i, 'linear_j': linear_j}
    _L0_gnn_all = _L0_gnn_setup()
    _L0_gnn_in = {k: v for k, v in _L0_gnn_all.items() if k in ('weight', 'linear_i', 'linear_j', )}
    del _L0_gnn_all

    def _L1_gnn_setup():
        import jax, jax.numpy as jnp
        import numpy as np
        N = 4096
        INPUT_DIM = 512
        KEY_DIM = 64
        OUT_DIM = 512
        N_HEADS = 8
        IDENTITY_BIAS = 0.01
        MASK_VAL = 1e+16

        def _xavier(key, shape, gain=np.sqrt(2.0)):
            std = gain * np.sqrt(2.0 / (shape[-2] + shape[-1]))
            return jax.random.normal(key, shape, dtype=jnp.float32) * np.float32(std)
        key = jax.random.key(seed)
        kx, ka, kk, kq, kv, ko = jax.random.split(key, 6)
        node_matrix = jax.random.normal(kx, (N, INPUT_DIM), dtype=jnp.float32)
        adjacency_matrix = jax.random.bernoulli(ka, 0.01, (N, N)).astype(jnp.float32)
        Wks = _xavier(kk, (N_HEADS, INPUT_DIM, KEY_DIM))
        Wqs = _xavier(kq, (N_HEADS, INPUT_DIM, KEY_DIM))
        Wvs = _xavier(kv, (N_HEADS, INPUT_DIM, KEY_DIM))
        Wo = _xavier(ko, (N_HEADS, KEY_DIM, OUT_DIM))
        return {'node_matrix': node_matrix, 'adjacency_matrix': adjacency_matrix, 'Wks': Wks, 'Wqs': Wqs, 'Wvs': Wvs, 'Wo': Wo}
    _L1_gnn_all = _L1_gnn_setup()
    _L1_gnn_in = {k: v for k, v in _L1_gnn_all.items() if k in ('Wks', 'Wqs', 'Wvs', 'Wo', )}
    del _L1_gnn_all

    return {
        "x": x,
        "adj": adj,
        "L0_gnn_weight": _L0_gnn_in["weight"],
        "L0_gnn_linear_i": _L0_gnn_in["linear_i"],
        "L0_gnn_linear_j": _L0_gnn_in["linear_j"],
        "L1_gnn_Wks": _L1_gnn_in["Wks"],
        "L1_gnn_Wqs": _L1_gnn_in["Wqs"],
        "L1_gnn_Wvs": _L1_gnn_in["Wvs"],
        "L1_gnn_Wo": _L1_gnn_in["Wo"],
    }

def reference(x, adj, L0_gnn_weight, L0_gnn_linear_i, L0_gnn_linear_j, L1_gnn_Wks, L1_gnn_Wqs, L1_gnn_Wvs, L1_gnn_Wo):
    import jax
    import jax.numpy as jnp
    def _L0_gnn_ref(x, adj, weight, linear_i, linear_j):
        import jax, jax.numpy as jnp
        import numpy as np
        NHEADS = 8
        OUT_FEATURES = 64
        ALPHA = 0.2
        NEG_INF = -10000000000.0
        n = x.shape[0]
        wh = (x @ weight).reshape(n, NHEADS, OUT_FEATURES)
        awh_i = (wh * linear_i).sum(axis=2)
        awh_j = (wh * linear_j).sum(axis=2)
        e = jax.nn.leaky_relu(awh_i[:, None, :] + awh_j[None, :, :], negative_slope=ALPHA)
        e = e + ((1.0 - adj) * NEG_INF)[:, :, None]
        a = jax.nn.softmax(e, axis=1)
        out = jnp.einsum('ijh,jhf->ihf', a, wh)
        return out.reshape(n, NHEADS * OUT_FEATURES)

    def _L1_gnn_ref(node_matrix, adjacency_matrix, Wks, Wqs, Wvs, Wo):
        import jax, jax.numpy as jnp
        import numpy as np
        N = 4096
        INPUT_DIM = 512
        KEY_DIM = 64
        OUT_DIM = 512
        N_HEADS = 8
        IDENTITY_BIAS = 0.01
        MASK_VAL = 1e+16

        def _xavier(key, shape, gain=np.sqrt(2.0)):
            std = gain * np.sqrt(2.0 / (shape[-2] + shape[-1]))
            return jax.random.normal(key, shape, dtype=jnp.float32) * np.float32(std)
        n = node_matrix.shape[0]
        kd = Wks.shape[-1]
        eye = jnp.eye(n, dtype=node_matrix.dtype)
        adj = jnp.maximum(adjacency_matrix, eye)
        q = jnp.einsum('nd,hdk->hnk', node_matrix, Wqs)
        k = jnp.einsum('nd,hdk->hnk', node_matrix, Wks)
        v = jnp.einsum('nd,hdk->hnk', node_matrix, Wvs)
        scores = jnp.einsum('hqk,hmk->hqm', q, k) * kd ** (-0.5)
        scores = scores + IDENTITY_BIAS * eye - MASK_VAL * (1.0 - adj)
        att = jax.nn.softmax(scores, axis=-1)
        return jnp.einsum('hqm,hmk,hko->qo', att, v, Wo)

    x = _layernorm(x + _L0_gnn_ref(x, adj, L0_gnn_weight, L0_gnn_linear_i, L0_gnn_linear_j), axis=-1)
    x = _layernorm(x + _L1_gnn_ref(x, adj, L1_gnn_Wks, L1_gnn_Wqs, L1_gnn_Wvs, L1_gnn_Wo), axis=-1)
    return x


_drawn_inputs = setup_inputs


def setup_inputs(seed=0):
    import zlib

    import numpy as np

    out = dict(_drawn_inputs(seed))
    spreads = {}
    factors = {}
    for name, (base, spread) in spreads.items():
        noise = np.random.default_rng([zlib.crc32(name.encode()), seed]).standard_normal(out[name].shape)
        drawn = base * np.exp(spread * noise) if base else spread * noise
        out[name] = jnp.asarray(drawn.astype(out[name].dtype))
    for name, factor in factors.items():
        out[name] = (out[name] * factor).astype(out[name].dtype)
    return out
```

```python
from contextlib import ExitStack

import numpy as np

import concourse.bass as bass
from concourse import mybir

F32 = mybir.dt.float32
BF16 = mybir.dt.bfloat16
F16 = mybir.dt.float16
ALU = mybir.AluOpType
ACT = mybir.ActivationFunctionType
X = mybir.AxisListType.X
ds = bass.ds

P = 128
N = 4096
D = 512
H = 8
F = D // H
KB = D // P
NT = N // P
CW = 512
C = N // CW
TC = CW // P
U = C * H
PIECES = N // CW
VG = 2 * F + 2
VA = 2 * F + 1
BIG = 2.0 ** 56
STEEP = 2.0 ** 60
VSCALE = 4096.0
PSHIFT = 44.0
SLOPE = 0.2
EPS = 1e-5
IDENTITY_BIAS = 0.01


class Chain:

    def __init__(self, eng, sem):
        self.eng, self.sem, self.base, self.n = eng, sem, 0, 0

    def at(self, base):
        self.base, self.n = base, 0

    def __call__(self, ins):
        self.n += 1
        ins.then_inc(self.sem, 1)
        self.eng.wait_ge(self.sem, self.base + self.n)


def gate(eng, passed):
    eng.sem_inc(passed, 1)


class Space:
    def __init__(self, nc, ctx, tag):
        self.nc, self.ctx, self.tag = nc, ctx, tag

    def sb(self, name, shape, dt):
        return self.ctx.enter_context(self.nc.sbuf_tensor(f"{self.tag}_{name}", shape, dt))

    def ps(self, name, shape, dt):
        return self.ctx.enter_context(self.nc.psum_tensor(f"{self.tag}_{name}", shape, dt))

    def sem(self, name):
        return self.ctx.enter_context(self.nc.semaphore(f"{self.tag}_{name}"))


def make_constants(nc, k):
    with ExitStack() as ctx:
        s = Space(nc, ctx, "c")
        made = s.sem("made")
        block = ctx.enter_context(nc.Block())

        @block.gpsimd
        def _(pool):
            nc.gpsimd.memset(k.identf[:], 0.0).then_inc(made, 1)
            pool.wait_ge(made, 1)
            nc.gpsimd.affine_select(out=k.identf[:], in_=k.identf[:], compare_op=ALU.not_equal, fill=1.0, base=0,
                                    pattern=[[-1, P]], channel_multiplier=1).then_inc(made, 1)
            nc.gpsimd.memset(k.negblk[:], -1.0).then_inc(made, 1)
            pool.wait_ge(made, 3)
            nc.gpsimd.affine_select(out=k.negblk[:], in_=k.negblk[:], compare_op=ALU.is_ge, fill=0.0, base=0,
                                    pattern=[[1, CW]], channel_multiplier=-P).then_inc(made, 1)
            pool.wait_ge(made, 4)
            nc.gpsimd.affine_select(out=k.negblk[:], in_=k.negblk[:], compare_op=ALU.is_ge, fill=0.0, base=P - 1,
                                    pattern=[[-1, CW]], channel_multiplier=P).then_inc(made, 1)
            pool.wait_ge(made, 5)

        @block.vector
        def _(dve):
            dve.wait_ge(made, 2)
            hi = float(np.float16(8 * IDENTITY_BIAS))
            nc.vector.tensor_copy(k.identb[:], k.identf[:])
            nc.vector.tensor_copy(k.identh[:], k.identf[:])
            nc.vector.tensor_scalar(k.negbig[:], k.identf[:], -BIG / 2, None, ALU.mult)
            nc.vector.tensor_scalar(k.bias_hi[:], k.identf[:], hi, None, ALU.mult)
            nc.vector.tensor_scalar(k.bias_lo[:], k.identf[:], 8 * IDENTITY_BIAS - hi, None, ALU.mult)
            nc.vector.tensor_scalar(k.offdiag[:], k.identf[:], -1.0, 1.0, ALU.mult, ALU.add)
            nc.vector.memset(k.ones[:], 1.0)


def project_gat(nc, k, x, weight, linear_i, linear_j, scr):
    with ExitStack() as ctx:
        s = Space(nc, ctx, "a")
        w = s.sb("w", [P, KB, D], F32)
        lin = s.sb("lin", [P, 2, D], F32)
        wl = s.sb("wl", [P, D], F32)
        w2 = s.sb("w2", [P, KB, 2 * H], F32)
        xs = s.sb("xs", [P, 2, TC, D], F32)
        xT = s.sb("xT", [P, 2, KB, CW], F32)
        wh = s.sb("wh", [P, NT, D], F32)
        aij = s.sb("aij", [P, NT, 2 * H], F32)
        aT = s.sb("aT", [2 * H, N], F32)
        top = s.sb("top", [P, 1], F32)
        topT = s.sb("topT", [2 * H, 1], F32)

        turned = s.ps("turned", [P, 2, D], F32)
        ps_wh = s.ps("ps_wh", [P, 2, D], F32)
        ps_a = s.ps("ps_a", [P, 2, 512], F32)
        ps_aT = s.ps("ps_aT", [2 * H, 1, CW], F32)

        loaded_w, loaded_x = s.sem("loaded_w"), [s.sem("loaded_x0"), s.sem("loaded_x1")]
        folded, chain = s.sem("folded"), s.sem("chain")
        t_done, t_copied = s.sem("t_done"), s.sem("t_copied")
        wh_done, wh_copied = s.sem("wh_done"), s.sem("wh_copied")
        aT_done, aT_copied = s.sem("aT_done"), s.sem("aT_copied")
        sum_done, topped, stored, wh_stored = s.sem("sum_done"), s.sem("topped"), s.sem("stored"), s.sem("wh_stored")
        block = ctx.enter_context(nc.Block())
        x_c = x.rearrange("(n p) d -> p n d", p=P)

        @block.sync
        def _(sp):
            sp.dma_start(w[:], weight.rearrange("(k p) n -> p k n", p=P)).then_inc(loaded_w, 16)
            for n, lin_dram in enumerate((linear_i, linear_j)):
                sp.dma_start(lin[:, n, :], lin_dram.rearrange("a h f -> (a h f)").partition_broadcast(P)).then_inc(loaded_w, 16)
            sp.dma_start(xs[:, 0], x_c[:, 0:TC, :]).then_inc(loaded_x[0], 16)
            sp.dma_start(xs[:, 1], x_c[:, TC:2 * TC, :]).then_inc(loaded_x[1], 16)
            with sp.Fori(0, C // 2 - 1) as i:
                for b in range(2):
                    sp.wait_ge(t_done, TC * (2 * i + b + 1))
                    sp.dma_start(xs[:, b], x_c[:, ds((2 * i + b + 2) * TC, TC), :]).then_inc(loaded_x[b], 16)
            sp.wait_ge(aT_copied, C + 1)
            sp.dma_start(scr.a_i[:, :], aT[0:H, :]).then_inc(stored, 16)
            sp.wait_ge(topped, 2)
            sp.dma_start(scr.top_a[:, :], topT[:]).then_inc(stored, 16)
            sp.dma_start(scr.top_wh[:, :], top[:]).then_inc(stored, 16)
            sp.wait_ge(stored, 48)

        @block.tensor
        def _(pe):
            def chunk(i, b):
                c = 2 * i + b
                pe.wait_ge(loaded_x[b], 16 * (i + 1))
                for t in range(TC):
                    pe.wait_ge(t_copied, TC * c + t + 1)
                    for kb in range(KB):
                        mm = pe.transpose(turned[:, t % 2, kb * P:(kb + 1) * P], xs[:, b, t, kb * P:(kb + 1) * P], k.identf[:])
                    mm.then_inc(t_done, 1)
                pe.wait_ge(t_copied, TC * (c + 1) + 2)
                for t in range(TC):
                    pe.wait_ge(wh_copied, 2 * (TC * c + t) + 1)
                    for kb in range(KB):
                        pe.matmul(ps_wh[:, t % 2, :], xT[:, b, kb, t * P:(t + 1) * P], w[:, kb, :], start=kb == 0, stop=kb == KB - 1)
                    for kb in range(KB):
                        mm = pe.matmul(ps_a[:, t % 2, 0:2 * H], xT[:, b, kb, t * P:(t + 1) * P], w2[:, kb, :],
                                       start=kb == 0, stop=kb == KB - 1)
                    mm.then_inc(wh_done, 1)
                pe.wait_ge(aT_copied, c + 1)
                for kb in range(KB):
                    mm = pe.matmul(ps_aT[:, 0, :], w2[:, kb, :], xT[:, b, kb, :], start=kb == 0, stop=kb == KB - 1)
                mm.then_inc(aT_done, 1)

            pe.wait_ge(loaded_w, 48)
            pe.wait_ge(folded, 1)
            with pe.Fori(0, C // 2) as i:
                chunk(i, 0)
                chunk(i, 1)
            pe.wait_ge(wh_copied, 2 * NT + 3)
            for t in range(NT):
                mm = pe.matmul(ps_wh[:, 0, :], k.ones[:], wh[:, t, :], start=t == 0, stop=t == NT - 1)
            mm.then_inc(sum_done, 1)

        @block.vector
        def _(dve):
            link = Chain(dve, chain)
            dve.sem_inc(t_copied, 2)
            dve.sem_inc(aT_copied, 1)
            dve.wait_ge(loaded_w, 48)
            for kb in range(KB):
                for n in range(2):
                    link(nc.vector.tensor_tensor(wl[:], w[:, kb, :], lin[:, n, :], ALU.mult))
                    link(nc.vector.tensor_reduce(w2[:, kb, n * H:(n + 1) * H], wl[:].rearrange("p (h f) -> p h f", f=F), X, ALU.add))
            nc.vector.tensor_copy(lin[:, 0, 0:1], lin[:, 0, 0:1]).then_inc(folded, 1)
            with dve.Fori(0, C // 2) as i:
                for b in range(2):
                    for t in range(TC):
                        dve.wait_ge(t_done, TC * (2 * i + b) + t + 1)
                        nc.vector.tensor_copy(xT[:, b, :, t * P:(t + 1) * P],
                                              turned[:, t % 2, :].rearrange("p (k n) -> p k n", k=KB)).then_inc(t_copied, 1)
                    dve.wait_ge(aT_done, 2 * i + b + 1)
                    nc.vector.tensor_copy(aT[:, ds((2 * i + b) * CW, CW)], ps_aT[:, 0, :]).then_inc(aT_copied, 1)
            dve.wait_ge(wh_copied, 2 * NT + 3)
            nc.vector.tensor_reduce(top[:], wh[:].rearrange("p t d -> p (t d)"), X, ALU.max,
                                    apply_absolute_value=True).then_inc(topped, 1)
            dve.wait_ge(aT_copied, C + 1)
            nc.vector.tensor_reduce(topT[:], aT[:], X, ALU.max).then_inc(topped, 1)
            dve.wait_ge(sum_done, 1)
            nc.vector.tensor_scalar(k.mean_wh[:], ps_wh[:, 0, :], 1.0 / N, None, ALU.mult)
            dve.wait_ge(wh_copied, 2 * NT + 3)
            nc.vector.tensor_copy(k.a_i[:], aij[:, :, 0:H])
            nc.vector.tensor_copy(k.a_j[:], aij[:, :, H:2 * H])

        @block.scalar
        def _(act):
            act.sem_inc(wh_copied, 3)
            with act.Fori(0, C // 2) as i:
                for b in range(2):
                    for t in range(TC):
                        n = TC * (2 * i + b) + t
                        act.wait_ge(wh_done, n + 1)
                        nc.scalar.copy(wh[:, ds(n, 1), :].rearrange("p a d -> p (a d)"), ps_wh[:, t % 2, :]).then_inc(wh_copied, 1)
                        nc.scalar.copy(aij[:, ds(n, 1), :].rearrange("p a d -> p (a d)"), ps_a[:, t % 2, 0:2 * H]).then_inc(wh_copied, 1)
            act.wait_ge(wh_copied, 2 * NT + 3)
            act.dma_start(scr.wh[:, :, :], wh[:]).then_inc(wh_stored, 16)
            act.wait_ge(wh_stored, 16)


def build_tables(nc, k, adj, scr):
    with ExitStack() as ctx:
        s = Space(nc, ctx, "b")
        tops = s.sb("tops", [P, P + 2 * H], F32)
        shift = s.sb("shift", [P, NT, H], F32)
        t1 = s.sb("t1", [P, NT, H], F32)
        t2 = s.sb("t2", [P, NT, H], F32)
        vf = s.sb("vf", [P, 2, NT, H], F32)
        vg = s.sb("vg", [P, 2, NT, H], F32)
        vh = s.sb("vh", [P, 2, NT, H], F16)
        vl = s.sb("vl", [P, 2, NT, H], F16)
        inv = s.sb("inv", [P, 1], F32)
        steep = s.sb("steep", [P, H, NT], F32)
        wh = s.sb("wh", [P, 4, D], F32)
        prod = s.sb("prod", [P, 4, D], F32)
        tab = s.sb("tab", [P, 2, H, 2, VG], F16)
        loaded, chain, exped = s.sem("loaded"), s.sem("chain"), s.sem("exped")
        ready = s.sem("ready")
        ld = [s.sem(f"ld{i}") for i in range(2)]
        mult, high, low, stored = s.sem("mult"), s.sem("high"), s.sem("low"), [s.sem("stored0"), s.sem("stored1")]
        st, passed = s.sem("st"), s.sem("passed")
        stage = s.sb("stage", [P, 4, TC, CW], F32)
        none = s.sb("none", [P, 2, TC, CW], BF16)
        rowm = s.sb("rowm", [P, 2, TC, CW], BF16)
        colm = s.sb("colm", [P, 2, TC, CW], BF16)
        turned = s.ps("turned", [P, 2, TC, CW], BF16)
        adj_in = [s.sem(f"adj_in{i}") for i in range(4)]
        cast, masked, t_done, copied = (s.sem(n) for n in ("cast", "masked", "t_done", "copied"))
        row_out = [s.sem("row_out0"), s.sem("row_out1")]
        col_out = [s.sem("col_out0"), s.sem("col_out1")]
        block = ctx.enter_context(nc.Block())
        G = C * C
        assert G // 4 == NT // 2
        adj_v = adj.rearrange("(t p) (g j) -> p t g j", p=P, j=CW)
        row_v = scr.row_mask.rearrange("(t p) (g j) -> p t g j", p=P, j=CW)
        col_v = scr.no_edge_T.rearrange("(t p) (g j) -> p t g j", p=P, j=CW)
        bc = lambda ap, n: ap.unsqueeze(3).to_broadcast([P, NT, H, n]) if n else ap

        @block.sync
        def _(sp):
            def place(g):
                return ((g >> 3) & (C - 1)) * TC, g & (C - 1)

            def load_group(g, b):
                row, col = place(g)
                sp.dma_start(stage[:, b], adj_v[:, ds(row, TC), ds(col, 1), :].rearrange("p t a j -> p t (a j)")).then_inc(adj_in[b], 16)

            def store_group(g, b):
                row, col = place(g)
                sp.wait_ge(masked, g + 1)
                gate(sp, passed)
                sp.dma_start(row_v[:, ds(row, TC), ds(col, 1), :].rearrange("p t a j -> p t (a j)"), rowm[:, b % 2]).then_inc(row_out[b % 2], 16)
                sp.wait_ge(copied, g + 1 + 2)
                gate(sp, passed)
                sp.dma_start(col_v[:, ds(col * TC, TC), ds((g >> 3) & (C - 1), 1), :].rearrange("p t a j -> p t (a j)"),
                             colm[:, b % 2]).then_inc(col_out[b % 2], 16)

            for g in range(4):
                load_group(g, g)
            sp.dma_start(tops[:, 0:P], scr.top_wh.rearrange("p a -> (p a)").partition_broadcast(P)).then_inc(loaded, 16)
            sp.dma_start(tops[:, P:P + 2 * H], scr.top_a.rearrange("p a -> (p a)").partition_broadcast(P)).then_inc(loaded, 16)
            for b in range(2):
                sp.dma_start(wh[:, b, :], scr.wh[:, b, :]).then_inc(ld[b], 16)
            sp.wait_ge(ready, 1)
            sp.dma_start(scr.steep[:, :, :].rearrange("h p t -> p h t"), steep[:]).then_inc(st, 16)

            def store(i, b):
                sp.wait_ge(low, 2 * (2 * i + b + 1))
                gate(sp, passed)
                sp.dma_start(scr.gat_v[:, :, ds(2 * i + b, 1), :].rearrange("h p a v -> p h (a v)"),
                             tab[:, b].rearrange("p h z v -> p h (z v)")).then_inc(stored[b], 16)

            def groups(i, more):
                for b in range(4):
                    store_group(4 * i + b, b)
                    if more:
                        load_group(4 * i + b + 4, b)

            with sp.Fori(0, NT // 2 - 1) as i:
                groups(i, True)
                for b in range(2):
                    sp.wait_ge(mult, 2 * (2 * i + b + 1))
                    gate(sp, passed)
                    sp.dma_start(wh[:, b, :], scr.wh[:, ds(2 * i + b + 2, 1), :].rearrange("p a d -> p (a d)")).then_inc(ld[b], 16)
                    store(i, b)
            groups(G // 4 - 1, False)
            for b in range(2):
                store(NT // 2 - 1, b)
            sp.wait_ge(st, 16)
            for b in range(2):
                sp.wait_ge(stored[b], 16 * (NT // 2 + 1))
                sp.wait_ge(row_out[b], 16 * (G // 2 + 1))
                sp.wait_ge(col_out[b], 16 * (G // 2 + 1))

        @block.vector
        def _(dve):
            link = Chain(dve, chain)
            dve.sem_inc(row_out[0], 16)
            dve.sem_inc(row_out[1], 16)
            dve.sem_inc(t_done, 2)
            dve.wait_ge(loaded, 32)
            link(nc.vector.tensor_reduce(k.top_wh[:], tops[:, 0:P], X, ALU.max))
            link(nc.vector.tensor_scalar(k.top_wh[:], k.top_wh[:], 1e-30, None, ALU.max))
            link(nc.vector.reciprocal(inv[:], k.top_wh[:]))
            m_j = tops[:, P + H:P + 2 * H].unsqueeze(1).to_broadcast([P, NT, H])
            link(nc.vector.tensor_tensor(shift[:], k.a_j[:], m_j, ALU.subtract))
            link(nc.vector.tensor_tensor(t1[:], k.a_i[:], m_j, ALU.add))
            link(nc.vector.tensor_scalar(t2[:], t1[:], SLOPE, None, ALU.mult))
            link(nc.vector.tensor_tensor(k.row_factors[:, :, :, 0], t1[:], t2[:], ALU.max))
            link(nc.vector.tensor_tensor(t1[:], t1[:], k.row_factors[:, :, :, 0], ALU.subtract))
            link(nc.vector.tensor_tensor(t2[:], t2[:], k.row_factors[:, :, :, 0], ALU.subtract))
            nc.vector.tensor_scalar(steep[:], k.a_j[:].rearrange("p t h -> p h t"), STEEP, None, ALU.mult).then_inc(ready, 1)
            dve.wait_ge(exped, 4)
            link(nc.vector.tensor_scalar(vf[:], vf[:], VSCALE, None, ALU.mult))
            odd = vf[:, 1].rearrange("p (a t) h -> p a t h", t=4)[:, :, 2:4, :]
            link(nc.vector.tensor_scalar(odd, odd, -1.0, None, ALU.mult))
            link(nc.vector.tensor_scalar(vg[:], vf[:], inv[:, 0:1], None, ALU.mult))
            link(nc.vector.tensor_copy(vh[:], vf[:]))
            link(nc.vector.tensor_tensor(vl[:], vf[:], vh[:], ALU.subtract))
            dve.sem_inc(ready, 1)
            with dve.Fori(0, NT // 2) as i:
                for b in range(4):
                    g = 4 * i + b
                    dve.wait_ge(adj_in[b], 16 * (i + 1))
                    dve.wait_ge(t_done, g + 1)
                    nc.vector.tensor_scalar(none[:, b % 2], stage[:, b], -2.0, 2.0, ALU.mult, ALU.add).then_inc(cast, 1)
                    dve.wait_ge(row_out[b % 2], 16 * (2 * i + b // 2 + 1))
                    nc.vector.tensor_scalar(rowm[:, b % 2], stage[:, b], BIG, -BIG, ALU.mult, ALU.add).then_inc(masked, 1)
                for b in range(2):
                    t = 2 * i + b
                    dve.wait_ge(ld[b], 16 * (i + 1))
                    for z in range(2):
                        nc.vector.tensor_tensor(prod[:, 2 * b + z, :].rearrange("p (h f) -> p h f", f=F),
                                                wh[:, b, :].rearrange("p (h f) -> p h f", f=F),
                                                vg[:, z, ds(t, 1), :].rearrange("p a h -> p h a").to_broadcast([P, H, F]),
                                                ALU.mult).then_inc(mult, 1)
                    for z in range(2):
                        dve.wait_ge(high, 2 * t + z + 1)
                        nc.vector.tensor_tensor(tab[:, b, :, z, F + 1:2 * F + 1], prod[:, 2 * b + z, :].rearrange("p (h f) -> p h f", f=F),
                                                tab[:, b, :, z, 0:F], ALU.subtract).then_inc(low, 1)

        @block.scalar
        def _(act):
            act.sem_inc(col_out[0], 16)
            act.sem_inc(col_out[1], 16)
            act.sem_inc(stored[0], 16)
            act.sem_inc(stored[1], 16)
            act.wait_ge(chain, 4)
            nc.scalar.activation(vf[:, 0], shift[:], ACT.Exp).then_inc(exped, 1)
            nc.scalar.activation(vf[:, 1], shift[:], ACT.Exp, scale=SLOPE).then_inc(exped, 1)
            act.wait_ge(chain, 9)
            nc.scalar.activation(k.row_factors[:, :, :, 0], t1[:], ACT.Exp).then_inc(exped, 1)
            nc.scalar.activation(k.row_factors[:, :, :, 1], t2[:], ACT.Exp).then_inc(exped, 1)
            act.wait_ge(ready, 2)
            with act.Fori(0, NT // 2) as i:
                for b in range(4):
                    g = 4 * i + b
                    act.wait_ge(t_done, g + 1 + 2)
                    act.wait_ge(col_out[b % 2], 16 * (2 * i + b // 2 + 1))
                    nc.scalar.copy(colm[:, b % 2], turned[:, b % 2]).then_inc(copied, 1)
                for b in range(2):
                    t = 2 * i + b
                    act.wait_ge(stored[b], 16 * (i + 1))
                    for z in range(2):
                        nc.scalar.copy(tab[:, b, :, z, F:F + 1], vh[:, z, ds(t, 1), :].rearrange("p a h -> p h a"))
                        nc.scalar.copy(tab[:, b, :, z, 2 * F + 1:VG], vl[:, z, ds(t, 1), :].rearrange("p a h -> p h a"))
                        act.wait_ge(mult, 2 * t + z + 1)
                        nc.scalar.copy(tab[:, b, :, z, 0:F], prod[:, 2 * b + z, :].rearrange("p (h f) -> p h f", f=F)).then_inc(high, 1)

        @block.tensor
        def _(pe):
            pe.sem_inc(copied, 2)
            with pe.Fori(0, G // 4) as i:
                for b in range(4):
                    g = 4 * i + b
                    pe.wait_ge(cast, g + 1)
                    pe.wait_ge(copied, g + 1)
                    for jt in range(TC):
                        for it in range(TC):
                            mm = pe.transpose(turned[:, b % 2, jt, it * P:(it + 1) * P],
                                              none[:, b % 2, it, jt * P:(jt + 1) * P], k.identb[:])
                    mm.then_inc(t_done, 1)


def gat(nc, k, x, scr):
    PAIRS = NT // 2
    RING = 8
    with ExitStack() as ctx:
        s = Space(nc, ctx, "g")
        strip = s.sb("strip", [P, NT, CW], BF16)
        vals = s.sb("vals", [P, 2, NT, 2 * VG], F16)
        steep = s.sb("steep", [P, 2, NT], F32)
        arow = s.sb("arow", [P, 2, CW], F32)
        minus_edges = s.sb("minus_edges", [P, PAIRS // 2, 2, CW], BF16)
        step = s.sb("step", [P, RING, 2, CW], BF16)
        pos = s.sb("pos", [P, RING, 2, CW], BF16)
        neg = s.sb("neg", [P, RING // 2, 2, CW], BF16)
        scaled = s.sb("scaled", [P, TC, 2, VG], F32)
        part = s.sb("part", [P, TC, 2, F + 1], F32)
        num = s.sb("num", [P, TC, H, F], F32)
        den = s.sb("den", [P, TC, H], F32)
        lone = s.sb("lone", [P, TC, H], F32)
        rden = s.sb("rden", [P, TC, H], F32)
        xs = s.sb("xs", [P, TC, D], F32)
        y = s.sb("y", [P, TC, D], F32)
        y2 = s.sb("y2", [P, TC, D], F32)
        bn = s.sb("bn", [P, TC, 6], F32)
        mv = s.sb("mv", [P, TC, 2], F32)
        acc = s.ps("acc", [P, 2, TC, 512], F32)

        vals_in = [[s.sem(f"vals_in{half}{b}") for b in range(2)] for half in range(2)]
        rows_in = [s.sem("rows_in0"), s.sem("rows_in1")]
        strip_in = [s.sem(f"strip_in{g}") for g in range(PIECES)]
        x_in, stepped, masked, multiplied = s.sem("x_in"), s.sem("stepped"), s.sem("masked"), s.sem("multiplied")
        chain, evac, den_ready, summed = s.sem("chain"), s.sem("evac"), s.sem("den_ready"), s.sem("summed")
        y_ready, y_normed, y_out = s.sem("y_ready"), s.sem("y_normed"), s.sem("y_out")
        pchain, x_used, passed = s.sem("pchain"), s.sem("x_used"), s.sem("passed")
        passed_p, passed_v = s.sem("passed_p"), s.sem("passed_v")
        block = ctx.enter_context(nc.Block())
        strip_v = scr.no_edge_T.rearrange("(g t p) i -> p g t i", p=P, g=PIECES)
        x_v = x.rearrange("(n p) d -> p n d", p=P)
        y_v = scr.y.rearrange("(n p) d -> p n d", p=P)

        @block.sync
        def _(sp):
            def load_half(h, b, half):
                tiles = slice(half * NT // 2, (half + 1) * NT // 2)
                sp.dma_start(vals[:, b, tiles], scr.gat_v[h, :, tiles, :]).then_inc(vals_in[half][b], 16)

            def load_rows(c, h, b):
                sp.dma_start(steep[:, b], scr.steep[h]).then_inc(rows_in[b], 16)
                sp.dma_start(arow[:, b], scr.a_i[h, ds(c * CW, CW)].partition_broadcast(P)).then_inc(rows_in[b], 16)

            def load_piece(at, g):
                sp.dma_start(strip[:, g * TC:(g + 1) * TC, :], strip_v[:, g, :, ds(at, CW)]).then_inc(strip_in[g], 16)

            def chunk(c, last):
                after = (c + 1) * CW if isinstance(c, int) else sp.snap((c + 1) * CW)
                for h in range(H):
                    u, b = c * H + h, h % 2
                    more = not (last and h >= H - 2)
                    for g in range(PIECES):
                        if h == H - 1 and not last:
                            sp.wait_ge(masked, RING + PAIRS * u + 2 * (g + 1))
                            gate(sp, passed)
                            load_piece(after, g)
                        if g == PIECES // 2 - 1 and more:
                            sp.wait_ge(multiplied, RING + PAIRS * u + PAIRS // 2)
                            load_half((h + 2) % H, b, 0)
                    if more:
                        sp.wait_ge(stepped, PAIRS * (u + 1))
                        load_rows(c + (h + 2) // H, (h + 2) % H, b)
                        sp.wait_ge(multiplied, RING + PAIRS * (u + 1))
                        load_half((h + 2) % H, b, 1)
                    if h == H - 1 and not last:
                        sp.wait_ge(x_used, c + 1)
                        sp.dma_start(xs[:], x_v[:, ds((c + 1) * TC, TC), :]).then_inc(x_in, 16)

            load_rows(0, 0, 0)
            load_piece(0, 0)
            load_half(0, 0, 0)
            load_half(0, 0, 1)
            for g in range(1, PIECES):
                load_piece(0, g)
            load_rows(0, 1, 1)
            for half in range(2):
                load_half(1, 1, half)
            sp.dma_start(xs[:], x_v[:, 0:TC, :]).then_inc(x_in, 16)
            with sp.Fori(0, C - 1) as c:
                chunk(c, False)
            chunk(C - 1, True)

        @block.scalar
        def _(act):
            with act.Fori(0, U // 2) as i:
                for b in range(2):
                    u = 2 * i + b
                    act.wait_ge(rows_in[b], 32 * (i + 1))
                    for j in range(PAIRS):
                        act.wait_ge(masked, PAIRS * u + j + 1)
                        for t in range(2):
                            ins = nc.scalar.activation(step[:, j % RING, t, :], arow[:, b, :], ACT.Sigmoid, scale=STEEP,
                                                       bias=steep[:, b, 2 * j + t:2 * j + t + 1])
                        ins.then_inc(stepped, 1)

        @block.vector
        def _(dve):
            link = Chain(dve, chain)
            EVAC = 3

            def evacuate(c, h, b):
                u = c * H + h
                dve.wait_ge(multiplied, RING + PAIRS * (u + 1))
                nc.vector.tensor_tensor(scaled[:], acc[:, b, :, 0:2 * VG].rearrange("p q (z v) -> p q z v", z=2),
                                        k.row_factors[:, ds(c * TC, TC), h, :].unsqueeze(3).to_broadcast([P, TC, 2, VG]),
                                        ALU.mult).then_inc(evac, 1)
                dve.wait_ge(evac, u + 1)
                link(nc.vector.tensor_tensor(part[:], scaled[:, :, :, 0:F + 1], scaled[:, :, :, F + 1:VG], ALU.add))
                if h == 0 and not (isinstance(c, int) and c == 0):
                    dve.wait_ge(summed, c)
                link(nc.vector.tensor_tensor(num[:, :, h, :], part[:, :, 0, 0:F], part[:, :, 1, 0:F], ALU.add))
                link(nc.vector.tensor_tensor(den[:, :, h:h + 1], part[:, :, 0, F:F + 1], part[:, :, 1, F:F + 1], ALU.add))

            def end_chunk(c):
                link(nc.vector.tensor_scalar(lone[:], den[:], 0.0, None, ALU.is_equal))
                link(nc.vector.tensor_tensor(den[:], den[:], lone[:], ALU.add))
                link(nc.vector.reciprocal(den[:], den[:]))
                nc.vector.tensor_scalar(rden[:], den[:], k.top_wh[:, 0:1], None, ALU.mult).then_inc(den_ready, 1)

            def norm_chunk(c):
                dve.wait_ge(y_ready, c + 1)
                for t in range(TC):
                    ins = nc.vector.bn_stats(bn[:, t, :], y2[:, t, :])
                link(ins)
                gate(dve, passed_v)
                for t in range(TC):
                    ins = nc.vector.bn_aggr(mv[:, t, :], bn[:, t, :])
                link(ins)
                nc.vector.tensor_copy(k.stats[:, ds(c * TC, TC), :], mv[:]).then_inc(y_normed, 1)

            def chunk(c, first):
                n = H * EVAC + 3 + 2
                link.at((c - 1) * n + (H - 1) * EVAC if not first else 0)
                for h in range(H):
                    for j in range(PAIRS):
                        p = PAIRS * (c * H + h) + j
                        if h == 0 and j % 2 == 0:
                            dve.wait_ge(strip_in[j // 2], 16 * (c + 1))
                        dve.wait_ge(stepped, p + 1)
                        if j % 2 == 0:
                            dve.wait_ge(multiplied, p + 2)
                        if j % 2 == 1 and h == 0:
                            nc.vector.tensor_scalar(minus_edges[:, j // 2], strip[:, 2 * j:2 * j + 2, :], 0.5, -1.0, ALU.mult, ALU.add)
                        ins = nc.vector.tensor_tensor(pos[:, j % RING], step[:, j % RING], strip[:, 2 * j:2 * j + 2, :], ALU.is_gt)
                        if j % 2 == 0:
                            ins = nc.vector.tensor_tensor(neg[:, j % RING // 2], step[:, j % RING], strip[:, 2 * j:2 * j + 2, :], ALU.is_equal)
                        ins.then_inc(masked, 1)
                        if j == 3 and h > 0:
                            evacuate(c, h - 1, (h - 1) % 2)
                        if j == 3 and h == 0 and not first:
                            evacuate(c - 1, H - 1, 1)
                            end_chunk(c - 1)
                        if j == 12 and h == 0 and not first:
                            norm_chunk(c - 1)

            dve.sem_inc(masked, RING)
            chunk(0, True)
            with dve.Fori(1, C) as c:
                chunk(c, False)
            link.at((C - 1) * (H * EVAC + 3 + 2) + (H - 1) * EVAC)
            evacuate(C - 1, H - 1, 1)
            end_chunk(C - 1)
            norm_chunk(C - 1)

        @block.tensor
        def _(pe):
            pe.sem_inc(multiplied, RING)

            def unit(u, i, b):
                for j in range(PAIRS):
                    if j % (PAIRS // 2) == 0:
                        pe.wait_ge(vals_in[j // (PAIRS // 2)][b], 16 * (i + 1))
                    pe.wait_ge(masked, RING + PAIRS * u + j + 1)
                    for t in range(2):
                        for it in range(TC):
                            rows = slice(it * P, (it + 1) * P)
                            if j % 2 == 0:
                                products = ((pos[:, j % RING, t, rows], 0, VG), (neg[:, j % RING // 2, t, rows], VG, 2 * VG))
                            else:
                                products = ((pos[:, j % RING, t, rows], 0, 2 * VG), (minus_edges[:, j // 2, t, rows], VG, 2 * VG))
                            for edges, lo, hi in products:
                                mm = pe.matmul(acc[:, b, it, lo:hi], edges, vals[:, b, 2 * j + t, lo:hi],
                                               start=j == 0 and t == 0 and lo == 0, stop=j == PAIRS - 1 and t == 1,
                                               skip_group_check=True)
                    mm.then_inc(multiplied, 1)

            unit(0, 0, 0)
            unit(1, 0, 1)
            with pe.Fori(1, U // 2) as i:
                for b in range(2):
                    pe.wait_ge(evac, 2 * i + b - 1)
                    unit(2 * i + b, i, b)

        @block.gpsimd
        def _(pool):
            def chunk(c, first):
                pool.wait_ge(den_ready, c + 1)
                if not first:
                    pool.wait_ge(y_normed, c)
                    pool.wait_ge(y_out, 16 * c)
                nc.gpsimd.tensor_tensor(y[:].rearrange("p t (h f) -> p (t h) f", f=F), num[:].rearrange("p t h f -> p (t h) f"),
                                        rden[:].rearrange("p t h -> p (t h)").unsqueeze(2).to_broadcast([P, TC * H, F]),
                                        ALU.mult).then_inc(pchain, 1)
                for t in range(TC):
                    nc.gpsimd.tensor_tensor(y2[:, t, :].rearrange("p (h f) -> p h f", f=F),
                                            lone[:, t, :].unsqueeze(2).to_broadcast([P, H, F]),
                                            k.mean_wh[:].rearrange("p (h f) -> p h f", f=F), ALU.mult).then_inc(pchain, 1)
                pool.wait_ge(pchain, (TC + 2) * c + TC + 1)
                pool.sem_inc(summed, 1)
                nc.gpsimd.tensor_tensor(y[:], y[:], y2[:], ALU.add).then_inc(pchain, 1)
                pool.wait_ge(pchain, (TC + 2) * (c + 1))
                pool.wait_ge(x_in, 16 * (c + 1))
                nc.gpsimd.tensor_tensor(y2[:], y[:], xs[:], ALU.add).then_inc(y_ready, 1)
                pool.wait_ge(y_ready, c + 1)
                pool.sem_inc(x_used, 1)
                pool.dma_start(y_v[:, ds(c * TC, TC), :], y2[:]).then_inc(y_out, 16)

            chunk(0, True)
            with pool.Fori(1, C) as c:
                chunk(c, False)
            pool.wait_ge(y_out, 16 * C)


def project_heads(nc, k, Wks, Wqs, Wvs, scr):
    with ExitStack() as ctx:
        s = Space(nc, ctx, "p")
        wq = s.sb("wq", [P, KB, H, F], F32)
        wk = s.sb("wk", [P, KB, H, F], F32)
        wv = s.sb("wv", [P, KB, H, F], F32)
        ys = s.sb("ys", [P, 2, TC, D], F32)
        xT = s.sb("xT", [P, KB, CW], F32)
        x1 = s.sb("x1", [P, 2, TC, D], F32)
        root = s.sb("root", [P, NT], F32)
        rstd = s.sb("rstd", [P, NT], F32)
        tmp = s.sb("tmp", [P, NT], F32)
        shift = s.sb("shift", [P, NT], F32)
        hi = s.sb("hi", [P, 4, CW], F16)
        lo = s.sb("lo", [P, 4, CW], F16)
        vv = s.sb("vv", [P, 2, H, TC, VA], F16)
        turned = s.ps("turned", [P, 2, D], F32)
        ps = s.ps("ps", [P, 4, CW], F32)
        w_in, y_in = s.sem("w_in"), [s.sem("y_in0"), s.sem("y_in1")]
        chain, rooted, normed, t_done, t_copied = s.sem("chain"), s.sem("rooted"), s.sem("normed"), s.sem("t_done"), s.sem("t_copied")
        done, high, low, ones_in, passed = (s.sem(n) for n in ("done", "high", "low", "ones_in", "passed"))
        out = [s.sem(f"out{b}") for b in range(4)]
        v_out = [s.sem("v_out0"), s.sem("v_out1")]
        x_out = [s.sem("x_out0"), s.sem("x_out1")]
        block = ctx.enter_context(nc.Block())
        y_v = scr.y.rearrange("(n p) d -> p n d", p=P)
        x1_v = scr.x1.rearrange("(n p) d -> p n d", p=P)
        GROUPS = 2 * KB + TC

        @block.sync
        def _(sp):
            sp.dma_start(ys[:, 0], y_v[:, 0:TC, :]).then_inc(y_in[0], 16)
            for w, src in ((wq, Wqs), (wk, Wks), (wv, Wvs)):
                for kb in range(KB):
                    sp.dma_start(w[:, kb], src[:, kb * P:(kb + 1) * P, :].rearrange("h p f -> p h f")).then_inc(w_in, 16)
            sp.dma_start(ys[:, 1], y_v[:, TC:2 * TC, :]).then_inc(y_in[1], 16)

            def chunk(i, b, more):
                c = 2 * i + b
                sp.wait_ge(normed, TC * (c + 1))
                gate(sp, passed)
                sp.dma_start(x1_v[:, ds(c * TC, TC), :], x1[:, b]).then_inc(x_out[b], 16)
                if more:
                    sp.dma_start(ys[:, b], y_v[:, ds((c + 2) * TC, TC), :]).then_inc(y_in[b], 16)
                for g in range(2 * KB):
                    sp.wait_ge(low, 4 + GROUPS * c + g + 1)
                    gate(sp, passed)
                    rows = slice((g % KB) * P, (g % KB + 1) * P)
                    if g < KB:
                        sp.dma_start(scr.q_hi[rows, ds(c * CW, CW)], hi[:, g % 4, :]).then_inc(out[g % 4], 16)
                        sp.dma_start(scr.q_lo[rows, ds(c * CW, CW)], lo[:, g % 4, :]).then_inc(out[g % 4], 16)
                    else:
                        for twice in range(2):
                            sp.dma_start(scr.k_hi[rows, ds(c * CW + twice * N, CW)], hi[:, g % 4, :]).then_inc(out[g % 4], 16)
                            sp.dma_start(scr.k_lo[rows, ds(c * CW + twice * N, CW)], lo[:, g % 4, :]).then_inc(out[g % 4], 16)
                sp.wait_ge(low, 4 + GROUPS * (c + 1))
                gate(sp, passed)
                for twice in range(2):
                    sp.dma_start(scr.v[:, :, ds(c * TC + twice * NT, TC), :].rearrange("h p t v -> p h (t v)"),
                                 vv[:, b].rearrange("p h t v -> p h (t v)")).then_inc(v_out[b], 16)

            with sp.Fori(0, C // 2 - 1) as i:
                for b in range(2):
                    chunk(i, b, True)
            for b in range(2):
                chunk(C // 2 - 1, b, False)
            for b in range(2):
                sp.wait_ge(x_out[b], 16 * (C // 2 + 1))
                sp.wait_ge(v_out[b], 32 * (C // 2 + 1))
            for b in range(4):
                sp.wait_ge(out[b], 96 * C + 64)

        @block.vector
        def _(dve):
            link = Chain(dve, chain)
            link(nc.vector.tensor_scalar(tmp[:], k.stats[:, :, 1], EPS, None, ALU.add))
            dve.wait_ge(rooted, 1)
            link(nc.vector.reciprocal(rstd[:], root[:]))
            link(nc.vector.tensor_tensor(root[:], rstd[:], rstd[:], ALU.mult))
            link(nc.vector.tensor_tensor(root[:], root[:], tmp[:], ALU.mult))
            link(nc.vector.tensor_scalar(root[:], root[:], -0.5, 1.5, ALU.mult, ALU.add))
            link(nc.vector.tensor_tensor(rstd[:], rstd[:], root[:], ALU.mult))
            link(nc.vector.memset(vv[:], 1.0))
            dve.sem_inc(ones_in, 1)
            for b in range(2):
                dve.sem_inc(x_out[b], 16)
            with dve.Fori(0, C // 2) as i:
                for b in range(2):
                    c = 2 * i + b
                    dve.wait_ge(y_in[b], 16 * (i + 1))
                    dve.wait_ge(x_out[b], 16 * (i + 1))
                    for t in range(TC):
                        nc.vector.tensor_scalar(x1[:, b, t, :], ys[:, b, t, :], k.stats[:, ds(c * TC + t, 1), 0:1].rearrange("p a s -> p (a s)"),
                                                rstd[:, ds(c * TC + t, 1)], ALU.subtract, ALU.mult).then_inc(normed, 1)
                    dve.wait_ge(done, GROUPS * c + 1)
                    for t in range(TC):
                        dve.wait_ge(t_done, TC * c + t + 1)
                        nc.vector.tensor_copy(xT[:, :, t * P:(t + 1) * P],
                                              turned[:, t % 2, :].rearrange("p (k n) -> p k n", k=KB)).then_inc(t_copied, 1)
                    for g in range(GROUPS):
                        dve.wait_ge(high, GROUPS * c + g + 1)
                        if g < 2 * KB:
                            nc.vector.tensor_tensor(lo[:, g % 4, :], ps[:, g % 4, :], hi[:, g % 4, :], ALU.subtract).then_inc(low, 1)
                        else:
                            t = g - 2 * KB
                            nc.vector.tensor_tensor(vv[:, b, :, t, 0:F], ps[:, g % 4, :].rearrange("p (h f) -> p h f", f=F),
                                                    vv[:, b, :, t, F:2 * F], ALU.subtract).then_inc(low, 1)

        @block.tensor
        def _(pe):
            pe.sem_inc(low, 4)
            pe.sem_inc(done, 1)
            pe.sem_inc(t_copied, 2)
            pe.wait_ge(w_in, 16 * 3 * KB)
            with pe.Fori(0, C // 2) as i:
                for b in range(2):
                    c = 2 * i + b
                    for t in range(TC):
                        pe.wait_ge(normed, TC * c + t + 1)
                        pe.wait_ge(t_copied, TC * c + t + 1)
                        for kb in range(KB):
                            mm = pe.transpose(turned[:, t % 2, kb * P:(kb + 1) * P], x1[:, b, t, kb * P:(kb + 1) * P], k.identf[:])
                        mm.then_inc(t_done, 1)
                    pe.wait_ge(t_copied, TC * (c + 1) + 2)
                    for g in range(GROUPS):
                        pe.wait_ge(low, GROUPS * c + g + 1)
                        for kb in range(KB):
                            if g < 2 * KB:
                                w, fb = (wq, wk)[g // KB], g % KB
                                mm = pe.matmul(ps[:, g % 4, :], w[:, kb, 2 * fb:2 * fb + 2, :].rearrange("p h f -> p (h f)"), xT[:, kb, :],
                                               start=kb == 0, stop=kb == KB - 1)
                            else:
                                t = g - 2 * KB
                                mm = pe.matmul(ps[:, g % 4, :], xT[:, kb, t * P:(t + 1) * P], wv[:, kb].rearrange("p h f -> p (h f)"),
                                               start=kb == 0, stop=kb == KB - 1)
                        mm.then_inc(done, 1)

        @block.scalar
        def _(act):
            act.wait_ge(chain, 1)
            nc.scalar.activation(root[:], tmp[:], ACT.Sqrt).then_inc(rooted, 1)
            for b in range(2):
                act.sem_inc(v_out[b], 32)
            for b in range(4):
                act.sem_inc(out[b], 64)
            act.wait_ge(ones_in, 1)
            with act.Fori(0, C // 2) as i:
                for b in range(2):
                    c = 2 * i + b
                    for g in range(GROUPS):
                        act.wait_ge(done, GROUPS * c + g + 2)
                        if g < KB:
                            act.wait_ge(out[g % 4], 96 * c + 64)
                            nc.scalar.copy(hi[:, g % 4, :], ps[:, g % 4, :]).then_inc(high, 1)
                        elif g < 2 * KB:
                            act.wait_ge(out[g % 4], 96 * c + 64 + 32)
                            nc.scalar.copy(hi[:, g % 4, :], ps[:, g % 4, :]).then_inc(high, 1)
                        else:
                            t = g - 2 * KB
                            if t == 0:
                                act.wait_ge(v_out[b], 32 * (i + 1))
                            nc.scalar.copy(vv[:, b, :, t, F:2 * F], ps[:, g % 4, :].rearrange("p (h f) -> p h f", f=F)).then_inc(high, 1)


def attend(nc, k, scr):
    WIDE = 2 * CW
    STEPS, ERING, SLOTS, TILES, LAG = NT // 2, 4, 3, TC * N // WIDE, 3
    ROWS_B = F + TC
    share = [2] + [1] * 6 + [2] + [1] * 6 + [0, 0]
    assert sum(share) == TILES and len(share) == STEPS
    with ExitStack() as ctx:
        s = Space(nc, ctx, "m")
        kA = s.sb("kA", [P, SLOTS, N], F16)
        kB = s.sb("kB", [P, SLOTS, N], F16)
        qA = s.sb("qA", [P, SLOTS, CW], F16)
        qB = s.sb("qB", [P, SLOTS, CW], F16)
        v = s.sb("v", [P, SLOTS, NT, VA], F16)
        strip = s.sb("strip", [P, NT, CW], BF16)
        rows = s.sb("rows", [P, TC, N], BF16)
        junk = s.sb("junk", [P, 2, WIDE], BF16)
        most = s.sb("most", [P, TC, N // WIDE], F32)
        cmax = s.sb("cmax", [P, TC], F32)
        e32 = s.sb("e32", [P, 2, 2 * CW], F32)
        ehi = s.sb("ehi", [P, ERING, 2 * CW], F16)
        elo = s.sb("elo", [P, ERING, 2 * CW], F16)
        got = s.sb("got", [P, 2, 2 * VA], F32)
        num = s.sb("num", [P, TC, F], F32)
        rden = s.sb("rden", [P, TC, 1], F32)
        o = s.sb("o", [P, TC, F], F32)
        scores = s.ps("scores", [P, 2, 2 * CW], F32)
        rough = s.ps("rough", [P, 2, CW], F32)
        acc = s.ps("acc", [P, 2, CW], F32)

        unit_in = [s.sem(f"unit_in{b}") for b in range(SLOTS)]
        strip_in = [s.sem(f"strip_in{g}") for g in range(PIECES)]
        rows_in = [s.sem(f"rows_in{g}") for g in range(PIECES)]
        ones_in, strip_fixed, rows_fixed = s.sem("ones_in"), s.sem("strip_fixed"), s.sem("rows_fixed")
        rough_done, max_taken, max_ready, max_turned = s.sem("rough_done"), s.sem("max_taken"), s.sem("max_ready"), s.sem("max_turned")
        scored, exped, low_done, multiplied = s.sem("scored"), s.sem("exped"), s.sem("low_done"), s.sem("multiplied")
        copied, got_used, chain, o_ready = s.sem("copied"), s.sem("got_used"), s.sem("chain"), s.sem("o_ready")
        o_out, passed, passed_p, passed_v = (s.sem(n) for n in ("o_out", "passed", "passed_p", "passed_v"))
        block = ctx.enter_context(nc.Block())
        strip_v = scr.no_edge_T.rearrange("(g t p) i -> p g t i", p=P, g=PIECES)
        rows_v = scr.row_mask.rearrange("(n p) m -> p n m", p=P)
        o_v = scr.o.rearrange("(n p) d -> p n d", p=P)
        TAKEN = TILES + 1

        @block.sync
        def _(sp):
            def place(u):
                c, h = (u >> 3) & (C - 1), u & (H - 1)
                where = (c * CW, h * F, c * TC, h)
                return where if isinstance(u, int) else tuple(sp.snap(w) for w in where)

            def load_unit(where, b):
                at, hf, tile, h = where
                for half in range(2):
                    sp.dma_start(kA[half * F:(half + 1) * F, b, :], scr.k_hi[ds(hf, F), ds(at, N)]).then_inc(unit_in[b], 16)
                sp.dma_start(qA[0:F, b, :], scr.q_hi[ds(hf, F), ds(at, CW)]).then_inc(unit_in[b], 16)
                sp.dma_start(qA[F:P, b, :], scr.q_lo[ds(hf, F), ds(at, CW)]).then_inc(unit_in[b], 16)
                sp.dma_start(qB[0:F, b, :], scr.q_hi[ds(hf, F), ds(at, CW)]).then_inc(unit_in[b], 16)
                sp.dma_start(kB[0:F, b, :], scr.k_lo[ds(hf, F), ds(at, N)]).then_inc(unit_in[b], 16)
                sp.dma_start(v[:, b], scr.v[ds(h, 1), :, ds(tile, NT), :].rearrange("a p t v -> p (a t) v")).then_inc(unit_in[b], 16)

            for u in range(SLOTS):
                load_unit(place(u), u)
            with sp.Fori(0, (U - SLOTS - 1) // SLOTS) as i:
                for b in range(SLOTS):
                    u = SLOTS * i + b
                    where = place(u + SLOTS)
                    sp.wait_ge(multiplied, STEPS * (u + 1))
                    gate(sp, passed)
                    load_unit(where, b)
            for u in range(U - 1 - SLOTS, U - SLOTS):
                sp.wait_ge(multiplied, STEPS * (u + 1))
                load_unit(place(u + SLOTS), u % SLOTS)

        @block.gpsimd
        def _(pool):
            def rows_piece(c, g):
                at = ((c + g) & (C - 1)) * CW if not isinstance(c, int) else (c + g) % C * CW
                pool.dma_start(rows[:, :, g * CW:(g + 1) * CW], rows_v[:, ds(c * TC, TC), ds(at, CW)]).then_inc(rows_in[g], 16)

            def strip_piece(c, g):
                piece = (c + g) & (C - 1) if not isinstance(c, int) else (c + g) % C
                pool.dma_start(strip[:, g * TC:(g + 1) * TC, :],
                               strip_v[:, ds(piece, 1), :, ds(c * CW, CW)].rearrange("p a t i -> p (a t) i")).then_inc(strip_in[g], 16)

            def fix(mask, arrived, done, c):
                pool.wait_ge(arrived, 16 * (c + 1))
                for t in range(TC):
                    ins = nc.gpsimd.tensor_tensor(mask[:, t, t * P:(t + 1) * P], mask[:, t, t * P:(t + 1) * P], k.offdiag[:], ALU.mult)
                    ins.then_inc(done, 1)

            nc.gpsimd.memset(kB[F:P, :, :], 1.0).then_inc(ones_in, 1)
            pool.wait_ge(ones_in, 1)
            for g in range(PIECES):
                rows_piece(0, g)
                strip_piece(0, g)
            fix(rows, rows_in[0], rows_fixed, 0)
            fix(strip, strip_in[0], strip_fixed, 0)
            with pool.Fori(1, C) as c:
                for g in range(PIECES):
                    pool.wait_ge(max_taken, TAKEN * (H * c - 1) + TC * (g * CW // WIDE + 1))
                    gate(pool, passed_p)
                    rows_piece(c, g)
                    if g == 0:
                        fix(rows, rows_in[0], rows_fixed, c)
                for g in range(PIECES):
                    pool.wait_ge(scored, STEPS * (H * c - 1) + 2 * (g + 1))
                    gate(pool, passed_p)
                    strip_piece(c, g)
                    if g == 0:
                        fix(strip, strip_in[0], strip_fixed, c)

        def unit_chunk(u):
            return u // H if isinstance(u, int) else (u >> 3) & (C - 1)

        @block.tensor
        def _(pe):
            def max_tile(u, b, n):
                if n >= 1:
                    pe.wait_ge(max_taken, TAKEN * u + n)
                for half in range(2):
                    at = n // TC * WIDE + half * CW
                    mm = pe.matmul(rough[:, half, :], qA[:, b, n % TC * P:(n % TC + 1) * P], kA[:, b, at:at + CW], start=True, stop=True)
                mm.then_inc(rough_done, 1)

            def turn_max(u):
                pe.wait_ge(max_ready, u + 1)
                pe.transpose(rough[0:TC, 0, 0:P], cmax[:], k.identf[:]).then_inc(max_turned, 1)

            def products(u, b, st):
                pe.wait_ge(low_done, STEPS * u + st + 1)
                if st == 0 and not (isinstance(u, int) and u == 0):
                    pe.wait_ge(copied, u)
                for t in range(2):
                    for q in range(TC):
                        for e, skip in ((ehi, 0), (elo, F)):
                            mm = pe.matmul(acc[:, q // 2, q % 2 * VA + skip:(q % 2 + 1) * VA], e[:, st % ERING, t * CW + q * P:t * CW + (q + 1) * P],
                                           v[:, b, 2 * st + t, skip:VA], start=st == 0 and t == 0 and q % 2 == 0 and e is ehi,
                                           stop=st == STEPS - 1 and t == 1, skip_group_check=True)
                mm.then_inc(multiplied, 1)

            def score(u, b, st):
                if not (isinstance(u, int) and u == 0 and st < 2):
                    pe.wait_ge(exped, STEPS * u + st - 1)
                if st == 0:
                    pe.wait_ge(max_taken, TAKEN * (u + 1))
                    pe.wait_ge(strip_fixed, TC * (unit_chunk(u) + 1))
                elif st % 2 == 0:
                    pe.wait_ge(strip_in[st // 2], 16 * (unit_chunk(u) + 1))
                for t in range(2):
                    m = 2 * st + t
                    to = scores[:, st % 2, t * CW:(t + 1) * CW]
                    pe.matmul(to, kA[:, b, m * P:(m + 1) * P], qA[:, b, :], start=True, stop=False, skip_group_check=True)
                    if m < TC:
                        for part in (k.bias_hi, k.bias_lo):
                            pe.matmul(to[:, m * P:(m + 1) * P], part[:], k.identh[:], start=False, stop=False, skip_group_check=True)
                    pe.matmul(to, k.negbig[:], strip[:, m, :], start=False, stop=False, skip_group_check=True)
                    mm = pe.matmul(to, kB[0:ROWS_B, b, m * P:(m + 1) * P], qB[0:ROWS_B, b, :], start=False, stop=True, skip_group_check=True)
                mm.then_inc(scored, 1)

            def unit(u, b, first=False, last=False, i=0):
                n = 0
                if not last:
                    pe.wait_ge(unit_in[(b + 1) % SLOTS], 16 * 7 * (i + (b + 1) // SLOTS + 1))
                for st in range(STEPS):
                    score(u, b, st)
                    if not last and share[st]:
                        max_tile(u + 1, (b + 1) % SLOTS, n)
                        n += 1
                    if st >= LAG:
                        products(u, b, st - LAG)
                    elif not first:
                        products(u - 1, (b - 1) % SLOTS, STEPS - LAG + st)
                    if not last and share[st] == 2:
                        max_tile(u + 1, (b + 1) % SLOTS, n)
                        n += 1
                    if st == STEPS - 2 and not last:
                        turn_max(u + 1)

            pe.wait_ge(unit_in[0], 16 * 7)
            pe.wait_ge(ones_in, 1)
            for n in range(TILES):
                max_tile(0, 0, n)
            turn_max(0)
            unit(0, 0, first=True)
            with pe.Fori(0, (U - 4) // SLOTS) as i:
                for j in range(SLOTS):
                    b = (1 + j) % SLOTS
                    unit(SLOTS * i + 1 + j, b, i=i + (1 + j) // SLOTS)
            for u in range(U - 3, U):
                unit(u, u % SLOTS, last=u == U - 1, i=u // SLOTS)
            for st in range(STEPS - LAG, STEPS):
                products(U - 1, (U - 1) % SLOTS, st)

        @block.scalar
        def _(act):
            def copy_out(u):
                act.wait_ge(multiplied, STEPS * (u + 1))
                act.wait_ge(got_used, u + 1)
                nc.scalar.copy(got[:], acc[:, :, 0:2 * VA]).then_inc(copied, 1)

            def store(u):
                act.wait_ge(o_ready, u + 1)
                c, h = (u // H, u % H) if isinstance(u, int) else ((u >> 3) & (C - 1), u & (H - 1))
                act.dma_start(o_v[:, ds(c * TC, TC), ds(h * F, F)], o[:]).then_inc(o_out, 16)

            def unit(u, first):
                for st in range(STEPS):
                    if st == 10 and not first:
                        store(u - 1)
                    act.wait_ge(scored, STEPS * u + st + 1)
                    if not (first and st < ERING):
                        act.wait_ge(multiplied, STEPS * u + st - ERING + 1)
                    nc.scalar.activation(ehi[:, st % ERING], scores[:, st % 2], ACT.Exp, scale=0.125)
                    if st == 2 and not first:
                        copy_out(u - 1)
                    if not (first and st < 2):
                        act.wait_ge(low_done, STEPS * u + st - 1)
                    nc.scalar.activation(e32[:, st % 2], scores[:, st % 2], ACT.Exp, scale=0.125).then_inc(exped, 1)

            act.sem_inc(got_used, 1)
            act.sem_inc(o_out, 16)
            unit(0, True)
            with act.Fori(1, U) as u:
                unit(u, False)
            copy_out(U - 1)
            store(U - 1)
            act.wait_ge(o_out, 16 * (U + 1))

        @block.vector
        def _(dve):
            link = Chain(dve, chain)

            def tile_there(u, n):
                if n == 0:
                    dve.wait_ge(rows_fixed, TC * (unit_chunk(u) + 1))
                elif n % TC == 0:
                    dve.wait_ge(rows_in[n // TC * 2], 16 * (unit_chunk(u) + 1))
                if n % TC == 0:
                    dve.wait_ge(rows_in[n // TC * 2 + 1], 16 * (unit_chunk(u) + 1))
                dve.wait_ge(rough_done, TILES * u + n + 1)

            def take_max(n):
                nc.vector.tensor_tensor_reduce(out=junk[:, n % 2], in0=rough[:].rearrange("p a m -> p (a m)"),
                                               in1=rows[:, n % TC, n // TC * WIDE:(n // TC + 1) * WIDE],
                                               scale=1.0, scalar=-3.0e38, op0=ALU.add, op1=ALU.max,
                                               accum_out=most[:, n % TC, n // TC:n // TC + 1]).then_inc(max_taken, 1)

            def reduce_max(u):
                dve.wait_ge(max_taken, TAKEN * u + TILES)
                nc.vector.tensor_reduce(cmax[:], most[:], X, ALU.max).then_inc(max_ready, 1)

            def place_max(u, b):
                dve.wait_ge(max_turned, u + 1)
                nc.vector.scalar_tensor_tensor(out=qB[F:F + TC, b, :].rearrange("p (a n) -> p a n", n=P),
                                               in0=rough[0:TC, 0:1, 0:P].to_broadcast([TC, TC, P]), scalar=-PSHIFT,
                                               in1=k.negblk[:].rearrange("p (a n) -> p a n", n=P),
                                               op0=ALU.add, op1=ALU.mult).then_inc(max_taken, 1)

            def evacuate(u):
                dve.wait_ge(copied, u + 1)
                g = got[:].rearrange("p a (q v) -> p (a q) v", v=VA)
                link(nc.vector.tensor_tensor(num[:], g[:, :, 0:F], g[:, :, F:2 * F], ALU.add))
                nc.vector.reciprocal(rden[:], g[:, :, 2 * F:VA]).then_inc(got_used, 1)
                dve.wait_ge(got_used, u + 2)
                dve.wait_ge(o_out, 16 * (u + 1))
                nc.vector.tensor_tensor(o[:], num[:], rden[:].to_broadcast([P, TC, F]), ALU.mult).then_inc(o_ready, 1)

            def low_part(u, st):
                dve.wait_ge(exped, STEPS * u + st + 1)
                nc.vector.tensor_tensor(elo[:, st % ERING], e32[:, st % 2], ehi[:, st % ERING], ALU.subtract).then_inc(low_done, 1)

            def unit(u, b, first=False, last=False):
                if not first:
                    link.at(u - 1)
                n = 0
                for st in range(STEPS):
                    if st == STEPS - 1 and not last:
                        place_max(u + 1, (b + 1) % SLOTS)
                    if st > 0:
                        low_part(u, st - 1)
                    elif not first:
                        low_part(u - 1, STEPS - 1)
                    if st == 5 and not first:
                        evacuate(u - 1)
                    if not last:
                        for m in range(share[st]):
                            tile_there(u + 1, n)
                            gate(dve, passed_v)
                            take_max(n)
                            n += 1
                        if n == TILES and share[st]:
                            reduce_max(u + 1)

            for n in range(TILES):
                tile_there(0, n)
                take_max(n)
            reduce_max(0)
            place_max(0, 0)
            unit(0, 0, first=True)
            with dve.Fori(0, (U - 4) // SLOTS) as i:
                for j in range(SLOTS):
                    unit(SLOTS * i + 1 + j, (1 + j) % SLOTS)
            for u in range(U - 3, U):
                unit(u, u % SLOTS, last=u == U - 1)
            low_part(U - 1, STEPS - 1)
            link.at(U - 1)
            evacuate(U - 1)


def finish(nc, k, Wo, scr, out):
    with ExitStack() as ctx:
        s = Space(nc, ctx, "f")
        wo = s.sb("wo", [P, KB, D], F32)
        os_ = s.sb("os", [P, 2, TC, D], F32)
        xs = s.sb("xs", [P, 2, TC, D], F32)
        oT = s.sb("oT", [P, 2, KB, P], F32)
        y = s.sb("y", [P, 2, TC, D], F32)
        z = s.sb("z", [P, 2, TC, D], F32)
        bn = s.sb("bn", [P, TC, 6], F32)
        mv = s.sb("mv", [P, TC, 2], F32)
        root = s.sb("root", [P, TC], F32)
        rstd = s.sb("rstd", [P, TC], F32)
        tmp = s.sb("tmp", [P, TC], F32)
        turned = s.ps("turned", [P, 2, D], F32)
        ps_y = s.ps("ps_y", [P, 2, D], F32)
        w_in, c_in = s.sem("w_in"), [s.sem("c_in0"), s.sem("c_in1")]
        t_done, t_copied, y_done, y_added = s.sem("t_done"), s.sem("t_copied"), s.sem("y_done"), s.sem("y_added")
        chain, var_ready, rooted, normed = s.sem("chain"), s.sem("var_ready"), s.sem("rooted"), s.sem("normed")
        z_out, passed, passed_v = [s.sem("z_out0"), s.sem("z_out1")], s.sem("passed"), s.sem("passed_v")
        block = ctx.enter_context(nc.Block())
        o_v = scr.o.rearrange("(n p) d -> p n d", p=P)
        x1_v = scr.x1.rearrange("(n p) d -> p n d", p=P)
        out_v = out.rearrange("(n p) d -> p n d", p=P)

        @block.sync
        def _(sp):
            def load(c, b):
                sp.dma_start(os_[:, b], o_v[:, ds(c * TC, TC), :]).then_inc(c_in[b], 16)
                sp.dma_start(xs[:, b], x1_v[:, ds(c * TC, TC), :]).then_inc(c_in[b], 16)

            sp.dma_start(wo[:], Wo.rearrange("h f d -> (h f) d").rearrange("(k p) d -> p k d", p=P)).then_inc(w_in, 16)
            load(0, 0)
            load(1, 1)

            def store(i, b):
                sp.wait_ge(normed, 2 * i + b + 1)
                gate(sp, passed)
                sp.dma_start(out_v[:, ds((2 * i + b) * TC, TC), :], z[:, b]).then_inc(z_out[b], 16)

            with sp.Fori(0, C // 2 - 1) as i:
                for b in range(2):
                    sp.wait_ge(y_added, TC * (2 * i + b + 1))
                    gate(sp, passed)
                    load(2 * i + b + 2, b)
                    store(i, b)
            for b in range(2):
                store(C // 2 - 1, b)
            for b in range(2):
                sp.wait_ge(z_out[b], 16 * (C // 2 + 1))

        @block.tensor
        def _(pe):
            pe.sem_inc(t_copied, 2)
            pe.wait_ge(w_in, 16)

            def tile(i, b, t, first=False):
                n = TC * (2 * i + b) + t
                pe.wait_ge(t_copied, n + 1)
                for kb in range(KB):
                    mm = pe.transpose(turned[:, t % 2, kb * P:(kb + 1) * P], os_[:, b, t, kb * P:(kb + 1) * P], k.identf[:])
                mm.then_inc(t_done, 1)
                pe.wait_ge(t_copied, n + 1 + 2)
                if not (first and b == 0 and t < 2):
                    pe.wait_ge(y_added, n - 1)
                for kb in range(KB):
                    mm = pe.matmul(ps_y[:, t % 2, :], oT[:, t % 2, kb, :], wo[:, kb, :], start=kb == 0, stop=kb == KB - 1)
                mm.then_inc(y_done, 1)

            def pair(i, first):
                for b in range(2):
                    pe.wait_ge(c_in[b], 32 * (i + 1))
                    for t in range(TC):
                        tile(i, b, t, first)

            pair(0, True)
            with pe.Fori(1, C // 2) as i:
                pair(i, False)

        @block.vector
        def _(dve):
            link = Chain(dve, chain)
            LINKS = 7
            dve.sem_inc(z_out[0], 16)
            dve.sem_inc(z_out[1], 16)
            with dve.Fori(0, C // 2) as i:
                for b in range(2):
                    c = 2 * i + b
                    link.at(c * LINKS)
                    dve.wait_ge(c_in[b], 32 * (i + 1))
                    for t in range(TC):
                        n = TC * c + t
                        dve.wait_ge(y_done, n + 1)
                        nc.vector.tensor_tensor(y[:, b, t, :], ps_y[:, t % 2, :], xs[:, b, t, :], ALU.add).then_inc(y_added, 1)
                        dve.wait_ge(y_added, n + 1)
                        ins = nc.vector.bn_stats(bn[:, t, :], y[:, b, t, :])
                    link(ins)
                    gate(dve, passed_v)
                    for t in range(TC):
                        ins = nc.vector.bn_aggr(mv[:, t, :], bn[:, t, :])
                    link(ins)
                    nc.vector.tensor_scalar(tmp[:], mv[:, :, 1], EPS, None, ALU.add).then_inc(var_ready, 1)
                    dve.wait_ge(rooted, c + 1)
                    link(nc.vector.reciprocal(rstd[:], root[:]))
                    link(nc.vector.tensor_tensor(root[:], rstd[:], rstd[:], ALU.mult))
                    link(nc.vector.tensor_tensor(root[:], root[:], tmp[:], ALU.mult))
                    link(nc.vector.tensor_scalar(root[:], root[:], -0.5, 1.5, ALU.mult, ALU.add))
                    link(nc.vector.tensor_tensor(rstd[:], rstd[:], root[:], ALU.mult))
                    dve.wait_ge(z_out[b], 16 * (i + 1))
                    for t in range(TC):
                        ins = nc.vector.tensor_scalar(z[:, b, t, :], y[:, b, t, :], mv[:, t, 0:1], rstd[:, t:t + 1],
                                                      ALU.subtract, ALU.mult)
                    ins.then_inc(normed, 1)

        @block.scalar
        def _(act):
            def turn(c, t):
                act.wait_ge(t_done, TC * c + t + 1)
                nc.scalar.copy(oT[:, t % 2], turned[:, t % 2, :].rearrange("p (k n) -> p k n", k=KB)).then_inc(t_copied, 1)

            def take_root(c):
                act.wait_ge(var_ready, c + 1)
                nc.scalar.activation(root[:], tmp[:], ACT.Sqrt).then_inc(rooted, 1)

            for t in range(TC):
                turn(0, t)
            with act.Fori(1, C) as c:
                turn(c, 0)
                take_root(c - 1)
                for t in range(1, TC):
                    turn(c, t)
            take_root(C - 1)


class Kept:
    pass


def build(nc, x, adj, weight, linear_i, linear_j, Wks, Wqs, Wvs, Wo, out):
    k, scr = Kept(), Kept()
    with ExitStack() as ctx:
        s = Space(nc, ctx, "k")

        def dram(name, shape, dt):
            return nc.dram_tensor(f"scr_{name}", shape, dt, kind="Internal").ap()

        k.identf = s.sb("identf", [P, P], F32)
        k.identb = s.sb("identb", [P, P], BF16)
        k.identh = s.sb("identh", [P, P], F16)
        k.negbig = s.sb("negbig", [P, P], BF16)
        k.bias_hi = s.sb("bias_hi", [P, P], F16)
        k.bias_lo = s.sb("bias_lo", [P, P], F16)
        k.offdiag = s.sb("offdiag", [P, P], BF16)
        k.ones = s.sb("ones", [P, P], F32)
        k.negblk = s.sb("negblk", [TC, CW], F32)
        k.mean_wh = s.sb("mean_wh", [P, D], F32)
        k.a_i = s.sb("a_i", [P, NT, H], F32)
        k.a_j = s.sb("a_j", [P, NT, H], F32)
        k.row_factors = s.sb("row_factors", [P, NT, H, 2], F32)
        k.top_wh = s.sb("top_wh", [P, 1], F32)
        k.stats = s.sb("stats", [P, NT, 2], F32)
        scr.a_i = dram("a_i", (H, N), F32)
        scr.top_a = dram("top_a", (2 * H, 1), F32)
        scr.top_wh = dram("top_wh", (P, 1), F32)
        scr.wh = dram("wh", (P, NT, D), F32)
        scr.steep = dram("steep", (H, P, NT), F32)
        scr.gat_v = dram("gat_v", (H, P, NT, 2 * VG), F16)
        scr.row_mask = dram("row_mask", (N, N), BF16)
        scr.no_edge_T = dram("no_edge_T", (N, N), BF16)
        scr.y = dram("y", (N, D), F32)
        scr.x1 = dram("x1", (N, D), F32)
        scr.q_hi = dram("q_hi", (D, N), F16)
        scr.q_lo = dram("q_lo", (D, N), F16)
        scr.k_hi = dram("k_hi", (D, 2 * N), F16)
        scr.k_lo = dram("k_lo", (D, 2 * N), F16)
        scr.v = dram("v", (H, P, 2 * NT, VA), F16)
        scr.o = dram("o", (N, D), F32)
        make_constants(nc, k)
        project_gat(nc, k, x, weight, linear_i, linear_j, scr)
        build_tables(nc, k, adj, scr)
        gat(nc, k, x, scr)
        project_heads(nc, k, Wks, Wqs, Wvs, scr)
        attend(nc, k, scr)
        finish(nc, k, Wo, scr, out)


_INS = ["x", "adj", "L0_gnn_weight", "L0_gnn_linear_i", "L0_gnn_linear_j", "L1_gnn_Wks", "L1_gnn_Wqs", "L1_gnn_Wvs", "L1_gnn_Wo"]


def kernel(**inputs):
    import concourse.bacc as _bacc
    from concourse.bass_utils import run_bass_kernel_spmd as _run

    nc = _bacc.Bacc("TRN2", target_bir_lowering=False, num_devices=1)
    arrays, args = {}, []
    for name in _INS:
        a = np.ascontiguousarray(inputs[name])
        arrays[f"in_{name}"] = a
        args.append(nc.dram_tensor(f"in_{name}", a.shape, mybir.dt.from_np(a.dtype), kind="ExternalInput").ap())
    args.append(nc.dram_tensor("out_0", (N, D), F32, kind="ExternalOutput").ap())
    build(nc, *args)
    return _run(nc, [arrays], core_ids=[0]).results[0]["out_0"]
```
